# Optimizing a Trainium2 kernel written in Bass

```python
import numpy as np
import jax
import jax.numpy as jnp

def _softmax(x, axis=-1):
    return jax.nn.softmax(x, axis=axis)

def _gelu(x):
    return jax.nn.gelu(x, approximate=True)

def _silu(x):
    return jax.nn.silu(x)

def _sigmoid(x):
    return jax.nn.sigmoid(x)

def _layernorm(x, axis=-1, eps=1e-05):
    m = jnp.mean(x, axis=axis, keepdims=True)
    v = jnp.var(x, axis=axis, keepdims=True)
    return (x - m) / jnp.sqrt(v + eps)

def _scatter_add(tgt, idx, src, axis=0):
    return tgt.at[idx].add(src)

def _segment_sum(src, seg, n):
    return jax.ops.segment_sum(src, seg, n)
kernel_name = 'mk_dlrm_tower_d1_rec_r8_aa4b4a'

def setup_inputs(seed: int=0):
    np.random.seed(seed)
    _w = jnp.asarray

    def _rec_inputs():
        import jax
        import jax.numpy as jnp
        _tk = jax.random.key(seed)
        dense_ctx = jax.random.normal(jax.random.fold_in(_tk, 190), (1024, 16), jnp.float32)
        ids = jnp.stack([jax.random.randint(jax.random.fold_in(_tk, 200 + f), (1024,), 0, v, jnp.int32) for f, v in enumerate([12500, 1000, 125000, 1250, 125000, 1250, 1000, 1250, 1000, 125000, 125000, 125000, 1000, 12500, 1250, 12500, 125000, 12500, 12500, 12500, 12500, 1000, 12500, 1000, 12500, 1250, 12500, 1000, 1250, 1250, 1250, 1250])], axis=1)
        tbl_0 = 0.05 * jax.random.normal(jax.random.fold_in(_tk, 500 + 0), (12500, 32), jnp.float32)
        tbl_1 = 0.05 * jax.random.normal(jax.random.fold_in(_tk, 500 + 1), (1000, 32), jnp.float32)
        tbl_2 = 0.05 * jax.random.normal(jax.random.fold_in(_tk, 500 + 2), (125000, 32), jnp.float32)
        tbl_3 = 0.05 * jax.random.normal(jax.random.fold_in(_tk, 500 + 3), (1250, 32), jnp.float32)
        tbl_4 = 0.05 * jax.random.normal(jax.random.fold_in(_tk, 500 + 4), (125000, 32), jnp.float32)
        tbl_5 = 0.05 * jax.random.normal(jax.random.fold_in(_tk, 500 + 5), (1250, 32), jnp.float32)
        tbl_6 = 0.05 * jax.random.normal(jax.random.fold_in(_tk, 500 + 6), (1000, 32), jnp.float32)
        tbl_7 = 0.05 * jax.random.normal(jax.random.fold_in(_tk, 500 + 7), (1250, 32), jnp.float32)
        tbl_8 = 0.05 * jax.random.normal(jax.random.fold_in(_tk, 500 + 8), (1000, 32), jnp.float32)
        tbl_9 = 0.05 * jax.random.normal(jax.random.fold_in(_tk, 500 + 9), (125000, 32), jnp.float32)
        tbl_10 = 0.05 * jax.random.normal(jax.random.fold_in(_tk, 500 + 10), (125000, 32), jnp.float32)
        tbl_11 = 0.05 * jax.random.normal(jax.random.fold_in(_tk, 500 + 11), (125000, 32), jnp.float32)
        tbl_12 = 0.05 * jax.random.normal(jax.random.fold_in(_tk, 500 + 12), (1000, 32), jnp.float32)
        tbl_13 = 0.05 * jax.random.normal(jax.random.fold_in(_tk, 500 + 13), (12500, 32), jnp.float32)
        tbl_14 = 0.05 * jax.random.normal(jax.random.fold_in(_tk, 500 + 14), (1250, 32), jnp.float32)
        tbl_15 = 0.05 * jax.random.normal(jax.random.fold_in(_tk, 500 + 15), (12500, 32), jnp.float32)
        tbl_16 = 0.05 * jax.random.normal(jax.random.fold_in(_tk, 500 + 16), (125000, 32), jnp.float32)
        tbl_17 = 0.05 * jax.random.normal(jax.random.fold_in(_tk, 500 + 17), (12500, 32), jnp.float32)
        tbl_18 = 0.05 * jax.random.normal(jax.random.fold_in(_tk, 500 + 18), (12500, 32), jnp.float32)
        tbl_19 = 0.05 * jax.random.normal(jax.random.fold_in(_tk, 500 + 19), (12500, 32), jnp.float32)
        tbl_20 = 0.05 * jax.random.normal(jax.random.fold_in(_tk, 500 + 20), (12500, 32), jnp.float32)
        tbl_21 = 0.05 * jax.random.normal(jax.random.fold_in(_tk, 500 + 21), (1000, 32), jnp.float32)
        tbl_22 = 0.05 * jax.random.normal(jax.random.fold_in(_tk, 500 + 22), (12500, 32), jnp.float32)
        tbl_23 = 0.05 * jax.random.normal(jax.random.fold_in(_tk, 500 + 23), (1000, 32), jnp.float32)
        tbl_24 = 0.05 * jax.random.normal(jax.random.fold_in(_tk, 500 + 24), (12500, 32), jnp.float32)
        tbl_25 = 0.05 * jax.random.normal(jax.random.fold_in(_tk, 500 + 25), (1250, 32), jnp.float32)
        tbl_26 = 0.05 * jax.random.normal(jax.random.fold_in(_tk, 500 + 26), (12500, 32), jnp.float32)
        tbl_27 = 0.05 * jax.random.normal(jax.random.fold_in(_tk, 500 + 27), (1000, 32), jnp.float32)
        tbl_28 = 0.05 * jax.random.normal(jax.random.fold_in(_tk, 500 + 28), (1250, 32), jnp.float32)
        tbl_29 = 0.05 * jax.random.normal(jax.random.fold_in(_tk, 500 + 29), (1250, 32), jnp.float32)
        tbl_30 = 0.05 * jax.random.normal(jax.random.fold_in(_tk, 500 + 30), (1250, 32), jnp.float32)
        tbl_31 = 0.05 * jax.random.normal(jax.random.fold_in(_tk, 500 + 31), (1250, 32), jnp.float32)
        _rk = jax.random.fold_in(_tk, 7)
        W_top1 = 0.0606339 * jax.random.normal(jax.random.fold_in(_tk, 801), (272, 512), jnp.float32)
        W_top2 = 0.0441942 * jax.random.normal(jax.random.fold_in(_tk, 802), (512, 256), jnp.float32)
        W_top3 = 0.0625 * jax.random.normal(jax.random.fold_in(_tk, 803), (256, 1), jnp.float32)
        b_top1 = jnp.zeros((512,), jnp.float32)
        b_top2 = jnp.zeros((256,), jnp.float32)
        return (dense_ctx, ids, tbl_0, tbl_1, tbl_2, tbl_3, tbl_4, tbl_5, tbl_6, tbl_7, tbl_8, tbl_9, tbl_10, tbl_11, tbl_12, tbl_13, tbl_14, tbl_15, tbl_16, tbl_17, tbl_18, tbl_19, tbl_20, tbl_21, tbl_22, tbl_23, tbl_24, tbl_25, tbl_26, tbl_27, tbl_28, tbl_29, tbl_30, tbl_31, W_top1, b_top1, W_top2, b_top2, W_top3)
    dense_ctx, ids, tbl_0, tbl_1, tbl_2, tbl_3, tbl_4, tbl_5, tbl_6, tbl_7, tbl_8, tbl_9, tbl_10, tbl_11, tbl_12, tbl_13, tbl_14, tbl_15, tbl_16, tbl_17, tbl_18, tbl_19, tbl_20, tbl_21, tbl_22, tbl_23, tbl_24, tbl_25, tbl_26, tbl_27, tbl_28, tbl_29, tbl_30, tbl_31, W_top1, b_top1, W_top2, b_top2, W_top3 = _rec_inputs()

    def _L0_rec_setup():
        import jax, jax.numpy as jnp
        import numpy as np
        B, F, D = (512, 32, 32)
        LAYER_SIZE = [128, 128]

        def _cin_forward(inputs, filters):
            x0 = inputs
            prev = inputs
            outs = []
            for W in filters:
                z = jnp.einsum('bhd,bmd->bhmd', x0, prev)
                b, h, m, d = z.shape
                z = z.reshape(b, h * m, d)
                cur = jnp.einsum('bpd,pn->bnd', z, W[0])
                cur = jax.nn.relu(cur)
                prev = cur
                outs.append(cur)
            result = jnp.concatenate(outs, axis=1)
            return jnp.sum(result, axis=-1)
        key = jax.random.key(seed)
        k1, k2, k3 = jax.random.split(key, 3)
        inputs = jax.random.normal(k1, (B, F, D), dtype=jnp.float32)
        field_nums = [F] + LAYER_SIZE
        filter_0 = jax.random.normal(k2, (1, field_nums[0] * field_nums[0], field_nums[1]), dtype=jnp.float32) * 0.05
        filter_1 = jax.random.normal(k3, (1, field_nums[0] * field_nums[1], field_nums[2]), dtype=jnp.float32) * 0.05
        return {'inputs': inputs, 'filter_0': filter_0, 'filter_1': filter_1}
    _L0_rec_all = _L0_rec_setup()
    _L0_rec_in = {k: v for k, v in _L0_rec_all.items() if k in ('filter_0', 'filter_1')}
    del _L0_rec_all
    return {'dense_ctx': dense_ctx, 'ids': ids, 'tbl_0': tbl_0, 'tbl_1': tbl_1, 'tbl_2': tbl_2, 'tbl_3': tbl_3, 'tbl_4': tbl_4, 'tbl_5': tbl_5, 'tbl_6': tbl_6, 'tbl_7': tbl_7, 'tbl_8': tbl_8, 'tbl_9': tbl_9, 'tbl_10': tbl_10, 'tbl_11': tbl_11, 'tbl_12': tbl_12, 'tbl_13': tbl_13, 'tbl_14': tbl_14, 'tbl_15': tbl_15, 'tbl_16': tbl_16, 'tbl_17': tbl_17, 'tbl_18': tbl_18, 'tbl_19': tbl_19, 'tbl_20': tbl_20, 'tbl_21': tbl_21, 'tbl_22': tbl_22, 'tbl_23': tbl_23, 'tbl_24': tbl_24, 'tbl_25': tbl_25, 'tbl_26': tbl_26, 'tbl_27': tbl_27, 'tbl_28': tbl_28, 'tbl_29': tbl_29, 'tbl_30': tbl_30, 'tbl_31': tbl_31, 'W_top1': W_top1, 'b_top1': b_top1, 'W_top2': W_top2, 'b_top2': b_top2, 'W_top3': W_top3, 'L0_rec_filter_0': _L0_rec_in['filter_0'], 'L0_rec_filter_1': _L0_rec_in['filter_1']}

def reference(dense_ctx, ids, tbl_0, tbl_1, tbl_2, tbl_3, tbl_4, tbl_5, tbl_6, tbl_7, tbl_8, tbl_9, tbl_10, tbl_11, tbl_12, tbl_13, tbl_14, tbl_15, tbl_16, tbl_17, tbl_18, tbl_19, tbl_20, tbl_21, tbl_22, tbl_23, tbl_24, tbl_25, tbl_26, tbl_27, tbl_28, tbl_29, tbl_30, tbl_31, W_top1, b_top1, W_top2, b_top2, W_top3, L0_rec_filter_0, L0_rec_filter_1):
    import jax
    import jax.numpy as jnp

    def _L0_rec_ref(inputs, filter_0, filter_1):
        import jax, jax.numpy as jnp
        import numpy as np
        B, F, D = (512, 32, 32)
        LAYER_SIZE = [128, 128]

        def _cin_forward(inputs, filters):
            x0 = inputs
            prev = inputs
            outs = []
            for W in filters:
                z = jnp.einsum('bhd,bmd->bhmd', x0, prev)
                b, h, m, d = z.shape
                z = z.reshape(b, h * m, d)
                cur = jnp.einsum('bpd,pn->bnd', z, W[0])
                cur = jax.nn.relu(cur)
                prev = cur
                outs.append(cur)
            result = jnp.concatenate(outs, axis=1)
            return jnp.sum(result, axis=-1)
        return _cin_forward(inputs, (filter_0, filter_1))
    e = jnp.stack([tbl_0[ids[:, 0]], tbl_1[ids[:, 1]], tbl_2[ids[:, 2]], tbl_3[ids[:, 3]], tbl_4[ids[:, 4]], tbl_5[ids[:, 5]], tbl_6[ids[:, 6]], tbl_7[ids[:, 7]], tbl_8[ids[:, 8]], tbl_9[ids[:, 9]], tbl_10[ids[:, 10]], tbl_11[ids[:, 11]], tbl_12[ids[:, 12]], tbl_13[ids[:, 13]], tbl_14[ids[:, 14]], tbl_15[ids[:, 15]], tbl_16[ids[:, 16]], tbl_17[ids[:, 17]], tbl_18[ids[:, 18]], tbl_19[ids[:, 19]], tbl_20[ids[:, 20]], tbl_21[ids[:, 21]], tbl_22[ids[:, 22]], tbl_23[ids[:, 23]], tbl_24[ids[:, 24]], tbl_25[ids[:, 25]], tbl_26[ids[:, 26]], tbl_27[ids[:, 27]], tbl_28[ids[:, 28]], tbl_29[ids[:, 29]], tbl_30[ids[:, 30]], tbl_31[ids[:, 31]]], axis=1)
    z = _L0_rec_ref(e, L0_rec_filter_0, L0_rec_filter_1)
    z = z.reshape(z.shape[0], -1)
    h = jnp.concatenate([z, dense_ctx], axis=1)
    h = jnp.maximum(h @ W_top1 + b_top1, 0.0)
    h = jnp.maximum(h @ W_top2 + b_top2, 0.0)
    y = h @ W_top3
    return y

_drawn_inputs = setup_inputs


def setup_inputs(seed=0):
    import zlib

    import numpy as np

    out = dict(_drawn_inputs(seed))
    spreads = {'b_top1': (0.0, 0.435), 'b_top2': (0.0, 0.436)}
    factors = {'tbl_0': 5.965,
     'tbl_1': 6.23,
     'tbl_2': 6.149,
     'tbl_3': 6.333,
     'tbl_4': 6.126,
     'tbl_5': 6.085,
     'tbl_6': 5.827,
     'tbl_7': 6.257,
     'tbl_8': 6.092,
     'tbl_9': 5.845,
     'tbl_10': 5.87,
     'tbl_11': 6.112,
     'tbl_12': 6.104,
     'tbl_13': 5.743,
     'tbl_14': 6.287,
     'tbl_15': 6.109,
     'tbl_16': 6.289,
     'tbl_17': 6.354,
     'tbl_18': 6.251,
     'tbl_19': 6.498,
     'tbl_20': 5.757,
     'tbl_21': 5.97,
     'tbl_22': 6.108,
     'tbl_23': 5.99,
     'tbl_24': 5.995,
     'tbl_25': 6.0,
     'tbl_26': 5.956,
     'tbl_27': 6.05,
     'tbl_28': 6.463,
     'tbl_29': 6.352,
     'tbl_30': 5.985,
     'tbl_31': 5.897,
     'L0_rec_filter_1': 8.0}
    for name, (base, spread) in spreads.items():
        noise = np.random.default_rng([zlib.crc32(name.encode()), seed]).standard_normal(out[name].shape)
        drawn = base * np.exp(spread * noise) if base else spread * noise
        out[name] = jnp.asarray(drawn.astype(out[name].dtype))
    for name, factor in factors.items():
        out[name] = (out[name] * factor).astype(out[name].dtype)
    return out
```

```python
from contextlib import ExitStack
from typing import NamedTuple

import numpy as np
import concourse.bass as bass
from concourse import mybir

P = 128
F32 = mybir.dt.float32
F32R = mybir.dt.float32r
I32 = mybir.dt.int32
U32 = mybir.dt.uint32
ALU = mybir.AluOpType
ACT = mybir.ActivationFunctionType
AX = mybir.AxisListType.X

FIELDS = 32
DIM = 32
BATCH = 1024
UNITS = 128
DENSE = 16
HID1, HID2 = 512, 256
BTILES = BATCH // P
QD = 4
QUADS = DIM // QD
ITERS = BTILES * QUADS
CYCLE = FIELDS + 1
LAST_SHIFT = CYCLE // 2
SHIFTS = P // FIELDS
CHUNKS = LAST_SHIFT // SHIFTS + 1
COPIES = 5
ROUNDS = CHUNKS + 1
GROUP = 4
STEPS = QD * FIELDS // GROUP
BANKS = STEPS // 2
TILE_BANKS = BANKS // QD
MACS = BANKS * GROUP
SLOTS = 8
POOL_OPS = 6
MLP_PE, MLP_ACT = 4, 9


class Quad(NamedTuple):
    n: object
    bt: object
    q: object
    prepares: bool
    mixes: bool
    sums: bool
    opens: bool
    closes: bool


def quads(engine):
    yield Quad(0, 0, 0, True, False, False, True, False)
    yield Quad(1, 0, 1, True, True, False, False, False)
    with engine.Fori(2, QUADS) as q:
        yield Quad(q, 0, q, True, True, True, False, False)
    with engine.Fori(1, BTILES) as bt:
        yield Quad(bt * QUADS, bt, 0, True, True, True, True, False)
        yield Quad(bt * QUADS + 1, bt, 1, True, True, True, False, True)
        with engine.Fori(2, QUADS) as q:
            yield Quad(bt * QUADS + q, bt, q, True, True, True, False, False)
    yield Quad(ITERS, BTILES, 0, False, True, True, True, False)
    yield Quad(ITERS + 1, BTILES, 1, False, False, True, False, True)


def wait(engine, semaphore, count):
    if isinstance(count, int) and count <= 0:
        return
    engine.wait_ge(semaphore, count)


def build_program(nc, dense, ids, tables, w1t, b1t, w2t, b2t, w3t, filter0, filter1, out):
    ctx = ExitStack()
    with ctx:
        def sb(name, shape, dt=F32):
            return ctx.enter_context(nc.sbuf_tensor(name, shape, dt))

        def ps(name):
            return ctx.enter_context(nc.psum_tensor(name, [P, 512], F32))

        def sem(name):
            return ctx.enter_context(nc.semaphore(name))

        ids_sb = sb("ids_sb", [P, BTILES, FIELDS], I32)
        idx_now = sb("idx_now", [P, FIELDS], I32)
        e_land = sb("e_land", [P, FIELDS, DIM])
        e_cur = sb("e_cur", [P, DIM, CYCLE])
        run32 = sb("run32", [P, QD, SHIFTS, FIELDS])
        run33 = sb("run33", [P, QD, COPIES, CYCLE])
        x0 = sb("x0", [P, QD, FIELDS])
        ident = sb("ident", [P, P])
        fold_a = sb("fold_a", [P, CHUNKS, UNITS])
        fold_b = sb("fold_b", [P, CHUNKS, UNITS])
        w0 = sb("w0", [P, CHUNKS, UNITS])
        base_t = sb("base_t", [P, 512])
        pairs = sb("pairs", [P, 2, 512])
        cur1 = sb("cur1", [P, 512])
        cur1_hi = sb("cur1_hi", [P, 512], F32R)
        cur1_lo = sb("cur1_lo", [P, 512], F32R)
        w1_raw = sb("w1_raw", [P, FIELDS * UNITS])
        w1_hi = sb("w1_hi", [P, FIELDS * UNITS], F32R)
        w1_lo = sb("w1_lo", [P, FIELDS * UNITS], F32R)
        mac = sb("mac", [P, 2, 2, UNITS])
        prod = sb("prod", [P, SLOTS, GROUP * UNITS])
        sum_a = sb("sum_a", [P, GROUP * UNITS])
        sum_b = sb("sum_b", [P, GROUP * UNITS])
        sum_c = sb("sum_c", [P, 2 * UNITS])
        sum_d = sb("sum_d", [P, 2 * UNITS])
        cur2 = sb("cur2", [P, QD, UNITS])
        acc1 = sb("acc1", [P, QD, P])
        acc2 = sb("acc2", [P, QD, UNITS])
        sum1 = sb("sum1", [P, P])
        sum2 = sb("sum2", [P, UNITS])
        dense_sb = sb("dense_sb", [P, BTILES, DENSE])
        dense_now = sb("dense_now", [P, DENSE])
        in2_t = sb("in2_t", [P, P])
        in3_t = sb("in3_t", [DENSE, P])
        top1 = sb("top1", [P, 2, HID1])
        top1_d = sb("top1_d", [DENSE, HID1])
        top2 = sb("top2", [P, HID1 // P, HID2])
        top3 = sb("top3", [P, HID2 // P])
        bias1 = sb("bias1", [P, HID1 // P])
        bias2 = sb("bias2", [P, HID2 // P])
        h1_t = sb("h1_t", [P, HID1 // P, P])
        h2_t = sb("h2_t", [P, HID2 // P, P])
        y_sb = sb("y_sb", [1, BATCH])

        mix = [ps(f"mix{i}") for i in range(4)]
        trans = [ps(f"trans{i}") for i in range(2)]
        cur1_ps = ps("cur1_ps")
        mlp_ps = ps("mlp_ps")

        ids_loaded = sem("ids_loaded")
        idx_ready = sem("idx_ready")
        gathered = sem("gathered")
        land_copied = sem("land_copied")
        fold_loaded = sem("fold_loaded")
        fold_zeroed = sem("fold_zeroed")
        zero_field = sem("zero_field")
        w0_ready = sem("w0_ready")
        w1_loaded = [sem(f"w1_loaded{i}") for i in range(4)]
        w1_hi_ready = sem("w1_hi_ready")
        w1_lo_ready = sem("w1_lo_ready")
        mlp_loaded = sem("mlp_loaded")
        dense_loaded = sem("dense_loaded")
        ident_steps = sem("ident_steps")
        quad_staged = sem("quad_staged")
        x0_staged = sem("x0_staged")
        transposed = sem("transposed")
        base_ready = sem("base_ready")
        pairs_ready = sem("pairs_ready")
        layer1_done = sem("layer1_done")
        cur1_ready = sem("cur1_ready")
        hi_ready = sem("hi_ready")
        lo_ready = sem("lo_ready")
        mix_done = sem("mix_done")
        macs_done = sem("macs_done")
        prods_done = sem("prods_done")
        pool_done = sem("pool_done")
        acc1_added = sem("acc1_added")
        acc1_closed = sem("acc1_closed")
        acc1_zeroed = sem("acc1_zeroed")
        acc2_added = sem("acc2_added")
        acc2_closed = sem("acc2_closed")
        acc2_zeroed = sem("acc2_zeroed")
        dense_ready = sem("dense_ready")
        mlp_pe = sem("mlp_pe")
        mlp_act = sem("mlp_act")
        stored = sem("stored")

        block = ctx.enter_context(nc.Block())

        w1_view = filter1[0].rearrange("(h m) n -> m h n", m=UNITS)
        w0_view = filter0[0]
        W1_PART = FIELDS * UNITS // 4

        def fold_loads():
            for shift in range(LAST_SHIFT + 1):
                t = shift // SHIFTS
                s = SHIFTS - 1 - shift % SHIFTS if t < CHUNKS - 1 else 0
                for m0, m1, turn in ((0, FIELDS - shift, 0), (CYCLE - shift, FIELDS, CYCLE)):
                    if m0 >= m1:
                        continue
                    a0 = (m0 + shift - turn) * FIELDS + m0
                    b0 = m0 * FIELDS + m0 + shift - turn
                    span = (m1 - m0 - 1) * (FIELDS + 1) + 1
                    rows = slice(FIELDS * s + m0, FIELDS * s + m1)
                    yield fold_a[rows, t, :], w0_view[a0:a0 + span:FIELDS + 1, :]
                    if shift:
                        yield fold_b[rows, t, :], w0_view[b0:b0 + span:FIELDS + 1, :]

        N_FOLD = len(list(fold_loads()))

        @block.sync
        def _(sp):
            sp.dma_start(ids_sb[:], ids.rearrange("(t p) f -> p t f", p=P)).then_inc(ids_loaded, 16)
            sp.wait_ge(fold_zeroed, 2)
            for dst, src in fold_loads():
                sp.dma_start(dst, src).then_inc(fold_loaded, 16)
            sp.dma_start(dense_sb[:], dense.rearrange("(t p) c -> p t c", p=P)).then_inc(dense_loaded, 16)
            sp.dma_start(top1[:], w1t[0:2 * P, :].rearrange("(k p) n -> p k n", p=P)).then_inc(mlp_loaded, 16)
            sp.dma_start(top1_d[:], w1t[2 * P:2 * P + DENSE, :]).then_inc(mlp_loaded, 16)
            sp.dma_start(top2[:], w2t.rearrange("(k p) n -> p k n", p=P)).then_inc(mlp_loaded, 16)
            with nc.allow_non_contiguous_dma(reason="a few hundred words"):
                sp.dma_start(top3[:], w3t.rearrange("(k p) o -> p (k o)", p=P)).then_inc(mlp_loaded, 16)
                sp.dma_start(bias1[:], b1t.rearrange("(k p) -> p k", p=P)).then_inc(mlp_loaded, 16)
                sp.dma_start(bias2[:], b2t.rearrange("(k p) -> p k", p=P)).then_inc(mlp_loaded, 16)
            sp.wait_ge(mlp_act, 1 + MLP_ACT * BTILES)
            sp.dma_start(out.rearrange("b o -> o b"), y_sb[:]).then_inc(stored, 16)
            sp.wait_ge(stored, 16)

        @block.gpsimd
        def _(pool):
            def set_indices(bt):
                nc.gpsimd.tensor_copy(idx_now[:], ids_sb[:, bt, :]).then_inc(idx_ready, 1)
                pool.wait_ge(idx_ready, bt + 1)

            def gather(f):
                nc.gpsimd.indirect_dma_start(
                    out=e_land[:, f, :], out_offset=None, in_=tables[f],
                    in_offset=bass.IndirectOffsetOnAxis(ap=idx_now[:, f:f + 1].bitcast(U32), axis=0),
                ).then_inc(gathered, 16)

            pool.wait_ge(ids_loaded, 16)
            set_indices(0)
            for f in range(FIELDS):
                gather(f)
            nc.gpsimd.memset(ident[:], 0.0).then_inc(ident_steps, 1)
            pool.wait_ge(ident_steps, 1)
            nc.gpsimd.affine_select(out=ident[:], in_=ident[:], compare_op=ALU.not_equal, fill=1.0,
                                    base=0, pattern=[[-1, P]], channel_multiplier=1).then_inc(ident_steps, 1)

            def add_products(quad, j):
                tile = (quad.n - 1) * QD + j
                ops = tile * POOL_OPS
                slot = [(j * TILE_BANKS + i) % SLOTS for i in range(TILE_BANKS)]
                wait(pool, pool_done, ops - POOL_OPS + 3)
                pool.wait_ge(prods_done, tile * 16 + 2 * GROUP)
                nc.gpsimd.tensor_tensor(sum_a[:], prod[:, slot[0], :], prod[:, slot[1], :],
                                        ALU.add).then_inc(pool_done, 1)
                pool.wait_ge(prods_done, tile * 16 + 4 * GROUP)
                nc.gpsimd.tensor_tensor(sum_b[:], prod[:, slot[2], :], prod[:, slot[3], :],
                                        ALU.add).then_inc(pool_done, 1)
                pool.wait_ge(pool_done, ops + 2)
                nc.gpsimd.tensor_tensor(sum_a[:], sum_a[:], sum_b[:], ALU.add).then_inc(pool_done, 1)
                pool.wait_ge(pool_done, ops + 3)
                nc.gpsimd.tensor_tensor(sum_c[:], sum_a[:, 0:2 * UNITS], sum_a[:, 2 * UNITS:],
                                        ALU.add).then_inc(pool_done, 1)
                pool.wait_ge(pool_done, ops + 4)
                pool.wait_ge(macs_done, (tile + 1) * 16)
                nc.gpsimd.tensor_tensor(sum_d[:], sum_c[:], mac[:, j % 2, :, :].rearrange("p a n -> p (a n)"),
                                        ALU.add).then_inc(pool_done, 1)
                pool.wait_ge(pool_done, ops + 5)
                if j == 0:
                    if not isinstance(quad.n, int) or quad.n > 1:
                        pool.wait_ge(acc2_added, quad.n)
                nc.gpsimd.tensor_tensor(cur2[:, j, :], sum_d[:, 0:UNITS], sum_d[:, UNITS:],
                                        ALU.add).then_inc(pool_done, 1)

            def mix_quad(quad, fields):
                for j in range(QD):
                    add_products(quad, j)
                    for f in fields[j::QD]:
                        gather(f)

            def mix_batch_tile(bt, gathers):
                for q in range(QUADS):
                    if gathers and q == 0:
                        pool.wait_ge(land_copied, bt + 1)
                        pool.wait_ge(gathered, 16 * FIELDS * (bt + 1))
                        set_indices(bt + 1)
                    fields = list(range(2 * q * QD, 2 * (q + 1) * QD)) if gathers and q < QUADS // 2 else []
                    mix_quad(Quad(bt * QUADS + q + 1, bt, q, True, True, True, False, False), fields)

            mix_batch_tile(0, True)
            with pool.Fori(1, BTILES - 1) as bt:
                mix_batch_tile(bt, True)
            mix_batch_tile(BTILES - 1, False)

        @block.scalar
        def _(act):
            for i in range(4):
                part = slice(i * W1_PART, (i + 1) * W1_PART)
                act.dma_start(w1_raw[:, part].rearrange("p (h n) -> p h n", n=UNITS),
                              w1_view[:, i * FIELDS // 4:(i + 1) * FIELDS // 4, :]).then_inc(w1_loaded[i], 16)
            for i in range(4):
                part = slice(i * W1_PART, (i + 1) * W1_PART)
                act.wait_ge(w1_loaded[i], 16)
                nc.scalar.activation(w1_hi[:, part], w1_raw[:, part], ACT.Copy).then_inc(w1_hi_ready, 1)
            act.sem_inc(mlp_act, 1)
            act.wait_ge(mlp_loaded, 16 * 6)

            def multiply(quad, a):
                n = quad.n
                bank = (n - 1) * BANKS + a
                j = a // TILE_BANKS
                if a == 0 or a == BANKS // 2:
                    act.wait_ge(x0_staged, 2 * n - 1 if a == 0 else 2 * n)
                act.wait_ge(mix_done, (n - 1) * STEPS + 2 * a + 2)
                wait(act, pool_done, ((n - 1) * QD + j - 2) * POOL_OPS + (1 if a % TILE_BANKS < 2 else 2))
                for i in range(GROUP):
                    h = (a % TILE_BANKS) * 2 * GROUP + GROUP + i
                    nc.scalar.activation(prod[:, a % SLOTS, i * UNITS:(i + 1) * UNITS],
                                         mix[(2 * a + 1) % 4][:, i * UNITS:(i + 1) * UNITS], ACT.Copy,
                                         scale=x0[:, j, h:h + 1]).then_inc(prods_done, 1)

            def split_high(n, half):
                act.wait_ge(cur1_ready, n + 1)
                wait(act, mix_done, (n - 1) * STEPS + (half + 1) * STEPS // 2)
                cols = slice(half * 256, half * 256 + 256)
                nc.scalar.activation(cur1_hi[:, cols], cur1[:, cols], ACT.Copy).then_inc(hi_ready, 1)

            def copy_base(n):
                act.wait_ge(transposed, n * ROUNDS + 1)
                wait(act, pairs_ready, n * CHUNKS)
                nc.scalar.activation(base_t[:], trans[0][:], ACT.Copy).then_inc(base_ready, 1)

            def finish_layer1(n):
                act.wait_ge(layer1_done, (n + 1) * CHUNKS)
                wait(act, lo_ready, 2 * n)
                wait(act, acc1_added, n)
                wait(act, hi_ready, 2 * n)
                nc.scalar.activation(cur1[:], cur1_ps[:], ACT.Relu).then_inc(cur1_ready, 1)
                split_high(n, 0)

            def mlp_stage(bt, k):
                u = bt - 1
                act.wait_ge(mlp_pe, 1 + u * MLP_PE + k + 1)
                if k == 0:
                    nc.scalar.activation(in2_t[:], mlp_ps[:, 0:P], ACT.Copy).then_inc(mlp_act, 1)
                    nc.scalar.activation(in3_t[:], mlp_ps[0:DENSE, P:2 * P], ACT.Copy).then_inc(mlp_act, 1)
                elif k == 1:
                    for c in range(HID1 // P):
                        nc.scalar.activation(h1_t[:, c, :], mlp_ps[:, c * P:(c + 1) * P], ACT.Relu,
                                             bias=bias1[:, c:c + 1]).then_inc(mlp_act, 1)
                elif k == 2:
                    for c in range(HID2 // P):
                        nc.scalar.activation(h2_t[:, c, :], mlp_ps[:, c * P:(c + 1) * P], ACT.Relu,
                                             bias=bias2[:, c:c + 1]).then_inc(mlp_act, 1)
                else:
                    nc.scalar.activation(y_sb[0:1, bass.ds(u * P, P)], mlp_ps[0:1, 0:P],
                                         ACT.Copy).then_inc(mlp_act, 1)

            for quad in quads(act):
                n = quad.n
                if not quad.mixes:
                    if quad.prepares:
                        copy_base(n)
                        finish_layer1(n)
                    else:
                        for k in range(MLP_PE):
                            mlp_stage(quad.bt, k)
                    continue
                for a in range(BANKS):
                    multiply(quad, a)
                    if a == 1:
                        split_high(n - 1, 1)
                    if quad.prepares and a == 3:
                        copy_base(n)
                    if quad.prepares and a == 11:
                        finish_layer1(n)
                    if quad.closes and a in (8, 10, 12, 14):
                        mlp_stage(quad.bt, (a - 8) // 2)

        @block.vector
        def _(dve):
            nc.vector.memset(fold_a[:], 0.0).then_inc(fold_zeroed, 1)
            nc.vector.memset(fold_b[:], 0.0).then_inc(fold_zeroed, 1)
            nc.vector.memset(acc1[:], 0.0).then_inc(acc1_zeroed, 1)
            nc.vector.memset(acc2[:], 0.0).then_inc(acc2_zeroed, 1)
            nc.vector.memset(e_cur[:, :, FIELDS], 0.0).then_inc(zero_field, 1)
            dve.sem_inc(acc2_added, 1)
            dve.wait_ge(fold_loaded, 16 * N_FOLD)
            nc.vector.tensor_tensor(w0[:, 0:4, :], fold_a[:, 0:4, :], fold_b[:, 0:4, :],
                                    ALU.add).then_inc(w0_ready, 1)
            nc.vector.tensor_tensor(w0[0:FIELDS, 4, :], fold_a[0:FIELDS, 4, :], fold_b[0:FIELDS, 4, :],
                                    ALU.add).then_inc(w0_ready, 1)
            for i in range(4):
                part = slice(i * W1_PART, (i + 1) * W1_PART)
                dve.wait_ge(w1_hi_ready, i + 1)
                nc.vector.tensor_tensor(w1_lo[:, part], w1_raw[:, part], w1_hi[:, part].bitcast(F32),
                                        ALU.subtract).then_inc(w1_lo_ready, 1)
            dve.wait_ge(dense_loaded, 16)

            def open_batch_tile(bt):
                dve.wait_ge(gathered, 16 * FIELDS * (bt + 1))
                wait(dve, quad_staged, 2 * bt * QUADS)
                nc.vector.tensor_copy(e_cur[:, :, 0:FIELDS],
                                      e_land[:].rearrange("p f d -> p d f")).then_inc(land_copied, 1)

            def stage_quad(quad):
                n = quad.n
                dve.wait_ge(land_copied, quad.bt + 1)
                wait(dve, transposed, n * ROUNDS)
                wait(dve, x0_staged, 2 * n)
                now = e_cur[:, bass.ds(quad.q * QD, QD), :].unsqueeze(2)
                nc.vector.tensor_copy(run32[:], now[:, :, :, 0:FIELDS].to_broadcast(
                    (P, QD, SHIFTS, FIELDS))).then_inc(quad_staged, 1)
                nc.vector.tensor_copy(run33[:], now.to_broadcast((P, QD, COPIES, CYCLE))).then_inc(quad_staged, 1)

            def stage_x0(n, half):
                dve.wait_ge(quad_staged, 2 * n + 1)
                wait(dve, prods_done, (n - 1) * MACS + (half + 1) * MACS // 2)
                wait(dve, macs_done, (n - 1) * MACS + (half + 1) * MACS // 2)
                nc.vector.tensor_copy(x0[:, 2 * half:2 * half + 2, :],
                                      run32[:, 2 * half:2 * half + 2, 0, :]).then_inc(x0_staged, 1)

            def multiply_pairs(n, t):
                rows = P if t < CHUNKS - 1 else FIELDS
                dve.wait_ge(transposed, n * ROUNDS + t + 2)
                if t == 0:
                    dve.wait_ge(base_ready, n + 1)
                wait(dve, layer1_done, n * CHUNKS + max(t - 1, 0))
                nc.vector.tensor_tensor(pairs[0:rows, t % 2, :], trans[(t + 1) % 2][0:rows, :],
                                        base_t[0:rows, :], ALU.mult).then_inc(pairs_ready, 1)

            def split_low(n, half):
                dve.wait_ge(hi_ready, 2 * n + half + 1)
                wait(dve, mix_done, (n - 1) * STEPS + (half + 1) * STEPS // 2)
                cols = slice(half * 256, half * 256 + 256)
                nc.vector.tensor_tensor(cur1_lo[:, cols], cur1[:, cols], cur1_hi[:, cols].bitcast(F32),
                                        ALU.subtract).then_inc(lo_ready, 1)

            def add_acc1(n, bt):
                dve.wait_ge(cur1_ready, n + 1)
                dve.wait_ge(acc1_zeroed, bt + 1)
                wait(dve, acc1_added, n)
                flat = acc1[:].rearrange("p j b -> p (j b)")
                nc.vector.tensor_tensor(flat, flat, cur1[:], ALU.add).then_inc(acc1_added, 1)

            def close_acc1(bt):
                dve.wait_ge(acc1_added, bt * QUADS)
                dve.wait_ge(mlp_pe, 1 + MLP_PE * (bt - 1))
                nc.vector.tensor_reduce(sum1[:], acc1[:].rearrange("p j b -> p b j"), AX,
                                        ALU.add).then_inc(acc1_closed, 1)
                if not isinstance(bt, int):
                    dve.wait_ge(acc1_closed, bt)
                    nc.vector.memset(acc1[:], 0.0).then_inc(acc1_zeroed, 1)

            def add_acc2(quad):
                n = quad.n
                dve.wait_ge(pool_done, (n - 1) * QD * POOL_OPS)
                dve.wait_ge(acc2_zeroed, quad.bt if quad.opens or quad.closes else quad.bt + 1)
                dve.wait_ge(acc2_added, n - 1)
                nc.vector.scalar_tensor_tensor(acc2[:], cur2[:], 0.0, acc2[:], ALU.max,
                                               ALU.add).then_inc(acc2_added, 1)

            def close_acc2(n, bt):
                dve.wait_ge(acc2_added, n)
                dve.wait_ge(mlp_pe, 1 + MLP_PE * (bt - 1))
                nc.vector.tensor_reduce(sum2[:], acc2[:].rearrange("p j n -> p n j"), AX,
                                        ALU.add).then_inc(acc2_closed, 1)
                nc.vector.tensor_copy(dense_now[:], dense_sb[:, bt - 1, :]).then_inc(dense_ready, 1)
                if not isinstance(bt, int):
                    dve.wait_ge(acc2_closed, bt)
                    nc.vector.memset(acc2[:], 0.0).then_inc(acc2_zeroed, 1)

            def multiply_add(n, e):
                j = e // TILE_BANKS
                if e == 0 or e == BANKS // 2:
                    dve.wait_ge(x0_staged, 2 * n - 1 if e == 0 else 2 * n)
                dve.wait_ge(mix_done, (n - 1) * STEPS + 2 * e + 1)
                if e % TILE_BANKS == 0:
                    wait(dve, pool_done, ((n - 1) * QD + j - 2) * POOL_OPS + 5)
                for i in range(GROUP):
                    k = (e % TILE_BANKS) * GROUP + i
                    h = (e % TILE_BANKS) * 2 * GROUP + i
                    src = mix[(2 * e) % 4][:, i * UNITS:(i + 1) * UNITS]
                    dst = mac[:, j % 2, i % 2, :]
                    scale = x0[:, j, h:h + 1]
                    if k < 2:
                        nc.vector.tensor_scalar(dst, src, scale, None, ALU.mult).then_inc(macs_done, 1)
                    else:
                        dve.wait_ge(macs_done, (n - 1) * MACS + e * GROUP + i - 1)
                        nc.vector.scalar_tensor_tensor(dst, src, scale, dst, ALU.mult,
                                                       ALU.add).then_inc(macs_done, 1)

            for quad in quads(dve):
                n = quad.n
                if not quad.mixes:
                    if quad.prepares:
                        open_batch_tile(0)
                        stage_quad(quad)
                        stage_x0(n, 0)
                        for t in range(CHUNKS):
                            multiply_pairs(n, t)
                        split_low(n, 0)
                        add_acc1(n, quad.bt)
                    else:
                        add_acc2(quad)
                        close_acc2(n, quad.bt)
                    continue
                for e in range(BANKS):
                    multiply_add(n, e)
                    if e == 1:
                        stage_x0(n - 1, 1)
                        if quad.opens:
                            if quad.prepares:
                                open_batch_tile(quad.bt)
                            close_acc1(quad.bt)
                        if quad.prepares:
                            stage_quad(quad)
                    if e == 2:
                        split_low(n - 1, 1)
                    if quad.sums and e == 6:
                        add_acc2(quad)
                        if quad.closes:
                            close_acc2(n, quad.bt)
                    if quad.prepares:
                        if e in (4, 6, 8, 9, 10):
                            multiply_pairs(n, (4, 6, 8, 9, 10).index(e))
                        if e == 13:
                            stage_x0(n, 0)
                            split_low(n, 0)
                        if e == 15:
                            add_acc1(n, quad.bt)

        @block.tensor
        def _(pe):
            def run(d, r):
                if r == 0:
                    return run32[:, d, :, :].rearrange("p s m -> p (s m)")
                start = SHIFTS * (r - 1) + SHIFTS - 1 if r < CHUNKS else LAST_SHIFT
                return run33[:, d, :, :].rearrange("p c f -> p (c f)")[:, start:start + (P if r < CHUNKS else FIELDS)]

            def transpose_round(n, r):
                if r == 0:
                    pe.wait_ge(quad_staged, 2 * n + 2)
                    wait(pe, pairs_ready, n * CHUNKS - 1)
                elif r == 1:
                    wait(pe, pairs_ready, n * CHUNKS)
                elif r == 2:
                    pe.wait_ge(base_ready, n + 1)
                else:
                    pe.wait_ge(pairs_ready, n * CHUNKS + r - 2)
                rows = FIELDS if r == CHUNKS else P
                for d in range(QD):
                    op = nc.tensor.transpose(trans[r % 2][0:rows, d * P:(d + 1) * P], run(d, r), ident[:])
                op.then_inc(transposed, 1)

            def layer1(n, t):
                rows = FIELDS if t == CHUNKS - 1 else P
                pe.wait_ge(pairs_ready, n * CHUNKS + t + 1)
                if t == 0:
                    wait(pe, cur1_ready, n)
                nc.tensor.matmul(cur1_ps[:], w0[0:rows, t, :], pairs[0:rows, t % 2, :],
                                 start=(t == 0), stop=(t == CHUNKS - 1)).then_inc(layer1_done, 1)

            def layer2(n, s):
                j, k = divmod(s, STEPS // QD)
                if k == 0 and j % 2 == 0:
                    pe.wait_ge(lo_ready, 2 * n - 1 if j == 0 else 2 * n)
                bank = (n - 1) * BANKS + s // 2
                wait(pe, prods_done if s % 2 else macs_done, (bank - 1) * GROUP)
                hi, lo = cur1_hi[:, j * P:(j + 1) * P], cur1_lo[:, j * P:(j + 1) * P]
                cols = slice(k * GROUP * UNITS, (k + 1) * GROUP * UNITS)
                nc.tensor.matmul(mix[s % 4][:], hi, w1_hi[:, cols], start=True, stop=False)
                nc.tensor.matmul(mix[s % 4][:], hi, w1_lo[:, cols], start=False, stop=False)
                nc.tensor.matmul(mix[s % 4][:], lo, w1_hi[:, cols], start=False, stop=True).then_inc(mix_done, 1)

            def mlp_stage(bt, k):
                u = bt - 1
                if k == 0:
                    pe.wait_ge(acc2_closed, bt)
                    pe.wait_ge(dense_ready, bt)
                    pe.wait_ge(mlp_act, 1 + u * MLP_ACT)
                    nc.tensor.transpose(mlp_ps[:, 0:P], sum2[:], ident[:])
                    nc.tensor.transpose(mlp_ps[0:DENSE, P:2 * P], dense_now[:], ident[:]).then_inc(mlp_pe, 1)
                elif k == 1:
                    pe.wait_ge(acc1_closed, bt)
                    pe.wait_ge(mlp_act, 1 + u * MLP_ACT + 2)
                    for c in range(HID1 // P):
                        cols = slice(c * P, (c + 1) * P)
                        nc.tensor.matmul(mlp_ps[:, cols], top1[:, 0, cols], sum1[:], start=True, stop=False)
                        nc.tensor.matmul(mlp_ps[:, cols], top1[:, 1, cols], in2_t[:], start=False, stop=False)
                        op = nc.tensor.matmul(mlp_ps[:, cols], top1_d[:, cols], in3_t[:], start=False, stop=True)
                    op.then_inc(mlp_pe, 1)
                elif k == 2:
                    pe.wait_ge(mlp_act, 1 + u * MLP_ACT + 6)
                    for c in range(HID2 // P):
                        cols = slice(c * P, (c + 1) * P)
                        for i in range(HID1 // P):
                            op = nc.tensor.matmul(mlp_ps[:, cols], top2[:, i, cols], h1_t[:, i, :],
                                                  start=(i == 0), stop=(i == HID1 // P - 1))
                    op.then_inc(mlp_pe, 1)
                else:
                    pe.wait_ge(mlp_act, 1 + u * MLP_ACT + 8)
                    for i in range(HID2 // P):
                        op = nc.tensor.matmul(mlp_ps[0:1, 0:P], top3[:, i:i + 1], h2_t[:, i, :],
                                              start=(i == 0), stop=(i == HID2 // P - 1))
                    op.then_inc(mlp_pe, 1)

            ROUND_AT = {6: 0, 7: 1, 10: 2, 13: 3, 16: 4, 19: 5}
            LAYER1_AT = {12: 0, 15: 1, 19: 2, 21: 3, 23: 4}
            MLP_AT = {17: 0, 20: 1, 24: 2, 28: 3}

            pe.sem_inc(mlp_pe, 1)
            pe.wait_ge(ident_steps, 2)
            for quad in quads(pe):
                n = quad.n
                if not quad.mixes:
                    if quad.prepares:
                        pe.wait_ge(w0_ready, 2)
                        for r in range(ROUNDS):
                            transpose_round(n, r)
                            if r >= 2:
                                layer1(n, r - 2)
                        layer1(n, CHUNKS - 1)
                        pe.wait_ge(w1_lo_ready, 4)
                        pe.wait_ge(mlp_loaded, 16 * 6)
                    else:
                        for k in range(MLP_PE):
                            mlp_stage(quad.bt, k)
                    continue
                for s in range(STEPS):
                    if quad.prepares and s in ROUND_AT:
                        transpose_round(n, ROUND_AT[s])
                    if quad.prepares and s in LAYER1_AT:
                        layer1(n, LAYER1_AT[s])
                    if quad.closes and s in MLP_AT:
                        mlp_stage(quad.bt, MLP_AT[s])
                    layer2(n, s)


def kernel(**inputs):
    import concourse.bacc as bacc
    from concourse.bass_utils import run_bass_kernel_spmd

    nc = bacc.Bacc("TRN2", target_bir_lowering=False, num_devices=1)
    names = (["dense_ctx", "ids"] + [f"tbl_{f}" for f in range(FIELDS)]
             + ["W_top1", "b_top1", "W_top2", "b_top2", "W_top3", "L0_rec_filter_0", "L0_rec_filter_1"])
    arrays, aps = {}, {}
    for name in names:
        a = np.ascontiguousarray(inputs[name])
        arrays[f"in_{name}"] = a
        aps[name] = nc.dram_tensor(f"in_{name}", a.shape, mybir.dt.from_np(a.dtype), kind="ExternalInput").ap()
    out = nc.dram_tensor("out_y", (BATCH, 1), F32, kind="ExternalOutput").ap()
    build_program(nc, aps["dense_ctx"], aps["ids"], [aps[f"tbl_{f}"] for f in range(FIELDS)],
                  aps["W_top1"], aps["b_top1"], aps["W_top2"], aps["b_top2"], aps["W_top3"],
                  aps["L0_rec_filter_0"], aps["L0_rec_filter_1"], out)
    result = run_bass_kernel_spmd(nc, [arrays], core_ids=[0])
    return result.results[0]["out_y"]
```

```python
from contextlib import ExitStack
from typing import NamedTuple

import numpy as np
import concourse.bass as bass
from concourse import mybir

P = 128
F32 = mybir.dt.float32
F32R = mybir.dt.float32r
I32 = mybir.dt.int32
U32 = mybir.dt.uint32
ALU = mybir.AluOpType
ACT = mybir.ActivationFunctionType
AX = mybir.AxisListType.X

FIELDS = 32
DIM = 32
BATCH = 1024
UNITS = 128
DENSE = 16
HID1, HID2 = 512, 256
BTILES = BATCH // P
QD = 4
QUADS = DIM // QD
ITERS = BTILES * QUADS
LAST_SHIFT = FIELDS // 2
SHIFTS = P // FIELDS
CHUNKS = LAST_SHIFT // SHIFTS + 1
LAST_ROWS = FIELDS // 2
ROUNDS = CHUNKS + 1
GROUP = 4
STEPS = QD * FIELDS // GROUP
BANKS = STEPS // 2
TILE_BANKS = BANKS // QD
MACS = BANKS * GROUP
SLOTS = 8
POOL_OPS = 6
MLP_PE, MLP_ACT = 4, 9


ROUND_AT = [8, 12, 14, 15, 18, 20]
LAYER1_AT = [18, 19, 20, 23, 25]
MLP_PE_AT = [24, 25, 28, 31]
X0_HIGH_AT, HIGH1_AT, ROUND_FIELDS_AT, ROUND_PAIRS_AT, X0_LOW_AT, FINISH_AT = 0, 2, 3, 6, 11, 12
MLP_ACT_AT = [11, 12, 14, 15]
OPEN_AT, LOW1_AT, SPLIT_AT, ACC2_AT, ACC1_AT, LOW0_AT, SPLIT_PAIRS_AT, CLOSE1_AT, CLOSE2_AT = 0, 2, 3, 4, 1, 12, 6, 9, 9
PAIRS_AT = [5, 6, 7, 8, 9]


class Quad(NamedTuple):
    n: object
    bt: object
    q: object
    prepares: bool
    mixes: bool
    sums: bool
    opens: bool
    closes: bool


def quads(engine):
    yield Quad(0, 0, 0, True, False, False, True, False)
    yield Quad(1, 0, 1, True, True, False, False, False)
    with engine.Fori(2, QUADS) as q:
        yield Quad(q, 0, q, True, True, True, False, False)
    with engine.Fori(1, BTILES) as bt:
        yield Quad(bt * QUADS, bt, 0, True, True, True, True, False)
        yield Quad(bt * QUADS + 1, bt, 1, True, True, True, False, True)
        with engine.Fori(2, QUADS) as q:
            yield Quad(bt * QUADS + q, bt, q, True, True, True, False, False)
    yield Quad(ITERS, BTILES, 0, False, True, True, True, False)
    yield Quad(ITERS + 1, BTILES, 1, False, False, True, False, True)


def wait(engine, semaphore, count):
    if isinstance(count, int) and count <= 0:
        return
    engine.wait_ge(semaphore, count)


def selection_matrices():
    s, m = np.divmod(np.arange(P), FIELDS)
    takes = [m + LAST_SHIFT] + [m + SHIFTS * t + s for t in range(CHUNKS - 1)]
    ones = np.arange(FIELDS)[:, None, None] == np.stack(takes)[None] % FIELDS
    return np.concatenate([ones, ones, 0 * ones, 0 * ones]).astype(np.float32)


def build_program(nc, dense, ids, tables, w1t, b1t, w2t, b2t, w3t, filter0, filter1, selection, out):
    ctx = ExitStack()
    with ctx:
        def sb(name, shape, dt=F32):
            return ctx.enter_context(nc.sbuf_tensor(name, shape, dt))

        def ps(name):
            return ctx.enter_context(nc.psum_tensor(name, [P, 512], F32))

        def sem(name):
            return ctx.enter_context(nc.semaphore(name))

        ids_sb = sb("ids_sb", [P, BTILES, FIELDS], I32)
        idx_now = sb("idx_now", [P, FIELDS], I32)
        e_land = sb("e_land", [P, FIELDS, DIM])
        e_cur = sb("e_cur", [P, DIM, FIELDS])
        e_quad = sb("e_quad", [P, QD, SHIFTS, FIELDS])
        parts = sb("parts", [P, 512], F32R)
        select_raw = sb("select_raw", [P, CHUNKS, P])
        select = sb("select", [P, CHUNKS, P], F32R)
        x0 = sb("x0", [P, QD, FIELDS])
        ident = sb("ident", [P, P])
        fold_a = sb("fold_a", [P, CHUNKS, UNITS])
        fold_b = sb("fold_b", [P, CHUNKS, UNITS])
        w0 = sb("w0", [P, CHUNKS, UNITS])
        w0_last = sb("w0_last", [P, UNITS], F32R)
        pair_parts = sb("pair_parts", [P, 512], F32R)
        base_t = sb("base_t", [P, 512])
        pairs = sb("pairs", [P, 2, 512])
        cur1 = sb("cur1", [P, 512])
        cur1_hi = sb("cur1_hi", [P, 512], F32R)
        cur1_lo = sb("cur1_lo", [P, 512], F32R)
        w1_raw = sb("w1_raw", [P, FIELDS * UNITS])
        w1_hi = sb("w1_hi", [P, FIELDS * UNITS], F32R)
        w1_lo = sb("w1_lo", [P, FIELDS * UNITS], F32R)
        mac = sb("mac", [P, 2, 2, UNITS])
        prod = sb("prod", [P, SLOTS, GROUP * UNITS])
        sum_a = sb("sum_a", [P, GROUP * UNITS])
        sum_c = sb("sum_c", [P, 2 * UNITS])
        cur2 = sb("cur2", [P, QD, UNITS])
        acc1 = sb("acc1", [P, QD, P])
        acc2 = sb("acc2", [P, QD, UNITS])
        sum1 = sb("sum1", [P, P])
        sum2 = sb("sum2", [P, UNITS])
        dense_sb = sb("dense_sb", [P, BTILES, DENSE])
        dense_now = sb("dense_now", [P, DENSE])
        in2_t = sb("in2_t", [P, P])
        in3_t = sb("in3_t", [DENSE, P])
        top1 = sb("top1", [P, 2, HID1])
        top1_d = sb("top1_d", [DENSE, HID1])
        top2 = sb("top2", [P, HID1 // P, HID2])
        top3 = sb("top3", [P, HID2 // P])
        bias1 = sb("bias1", [P, HID1 // P])
        bias2 = sb("bias2", [P, HID2 // P])
        h1_t = sb("h1_t", [P, HID1 // P, P])
        h2_t = sb("h2_t", [P, HID2 // P, P])
        y_sb = sb("y_sb", [1, BATCH])

        mix = [ps(f"mix{i}") for i in range(4)]
        trans = [ps(f"trans{i}") for i in range(2)]
        cur1_ps = ps("cur1_ps")
        mlp_ps = ps("mlp_ps")

        ids_loaded = sem("ids_loaded")
        idx_ready = sem("idx_ready")
        gathered = sem("gathered")
        land_copied = sem("land_copied")
        fold_loaded = sem("fold_loaded")
        fold_zeroed = sem("fold_zeroed")
        select_loaded = sem("select_loaded")
        select_ready = sem("select_ready")
        w0_ready = sem("w0_ready")
        w1_loaded = [sem(f"w1_loaded{i}") for i in range(4)]
        w1_hi_ready = sem("w1_hi_ready")
        w1_lo_ready = sem("w1_lo_ready")
        mlp_loaded = sem("mlp_loaded")
        dense_loaded = sem("dense_loaded")
        ident_steps = sem("ident_steps")
        quad_staged = sem("quad_staged")
        x0_staged = sem("x0_staged")
        transposed = sem("transposed")
        parts_high = sem("parts_high")
        parts_ready = sem("parts_ready")
        base_ready = sem("base_ready")
        pairs_ready = sem("pairs_ready")
        pairs_high = sem("pairs_high")
        pairs_split = sem("pairs_split")
        layer1_done = sem("layer1_done")
        cur1_ready = sem("cur1_ready")
        hi_ready = sem("hi_ready")
        lo_ready = sem("lo_ready")
        mix_done = sem("mix_done")
        macs_done = sem("macs_done")
        prods_done = sem("prods_done")
        pool_done = sem("pool_done")
        acc1_added = sem("acc1_added")
        acc1_closed = sem("acc1_closed")
        acc1_zeroed = sem("acc1_zeroed")
        acc2_added = sem("acc2_added")
        acc2_closed = sem("acc2_closed")
        acc2_zeroed = sem("acc2_zeroed")
        dense_ready = sem("dense_ready")
        mlp_pe = sem("mlp_pe")
        mlp_act = sem("mlp_act")
        stored = sem("stored")

        block = ctx.enter_context(nc.Block())

        w1_view = filter1[0].rearrange("(h m) n -> m h n", m=UNITS)
        w0_view = filter0[0]
        W1_PART = FIELDS * UNITS // 4

        def fold_loads():
            for shift in range(LAST_SHIFT + 1):
                t, s = divmod(shift, SHIFTS)
                last = shift == LAST_SHIFT
                t, count, blocks = (0, LAST_ROWS, (0, 1, 2)) if last else (t + 1, FIELDS, (s,))
                for m0, m1, turn in ((0, min(count, FIELDS - shift), 0), (FIELDS - shift, count, FIELDS)):
                    if m0 >= m1:
                        continue
                    a0 = (m0 + shift - turn) * FIELDS + m0
                    b0 = m0 * FIELDS + m0 + shift - turn
                    span = (m1 - m0 - 1) * (FIELDS + 1) + 1
                    for block in blocks:
                        rows = slice(FIELDS * block + m0, FIELDS * block + m1)
                        yield fold_a[rows, t, :], w0_view[a0:a0 + span:FIELDS + 1, :]
                        if shift:
                            yield fold_b[rows, t, :], w0_view[b0:b0 + span:FIELDS + 1, :]

        N_FOLD = len(list(fold_loads()))

        @block.sync
        def _(sp):
            sp.dma_start(ids_sb[:], ids.rearrange("(t p) f -> p t f", p=P)).then_inc(ids_loaded, 16)
            sp.dma_start(select_raw[:], selection).then_inc(select_loaded, 16)
            sp.wait_ge(fold_zeroed, 3)
            for dst, src in fold_loads():
                sp.dma_start(dst, src).then_inc(fold_loaded, 16)
            sp.dma_start(dense_sb[:], dense.rearrange("(t p) c -> p t c", p=P)).then_inc(dense_loaded, 16)
            sp.dma_start(top1[:], w1t[0:2 * P, :].rearrange("(k p) n -> p k n", p=P)).then_inc(mlp_loaded, 16)
            sp.dma_start(top1_d[:], w1t[2 * P:2 * P + DENSE, :]).then_inc(mlp_loaded, 16)
            sp.dma_start(top2[:], w2t.rearrange("(k p) n -> p k n", p=P)).then_inc(mlp_loaded, 16)
            with nc.allow_non_contiguous_dma(reason="a few hundred words"):
                sp.dma_start(top3[:], w3t.rearrange("(k p) o -> p (k o)", p=P)).then_inc(mlp_loaded, 16)
                sp.dma_start(bias1[:], b1t.rearrange("(k p) -> p k", p=P)).then_inc(mlp_loaded, 16)
                sp.dma_start(bias2[:], b2t.rearrange("(k p) -> p k", p=P)).then_inc(mlp_loaded, 16)
            sp.wait_ge(mlp_act, 1 + MLP_ACT * BTILES)
            sp.dma_start(out.rearrange("b o -> o b"), y_sb[:]).then_inc(stored, 16)
            sp.wait_ge(stored, 16)

        @block.gpsimd
        def _(pool):
            def set_indices(bt):
                nc.gpsimd.tensor_copy(idx_now[:], ids_sb[:, bt, :]).then_inc(idx_ready, 1)
                pool.wait_ge(idx_ready, bt + 1)

            def gather(f):
                nc.gpsimd.indirect_dma_start(
                    out=e_land[:, f, :], out_offset=None, in_=tables[f],
                    in_offset=bass.IndirectOffsetOnAxis(ap=idx_now[:, f:f + 1].bitcast(U32), axis=0),
                ).then_inc(gathered, 16)

            pool.wait_ge(ids_loaded, 16)
            set_indices(0)
            for f in range(FIELDS):
                gather(f)
            nc.gpsimd.memset(ident[:], 0.0).then_inc(ident_steps, 1)
            pool.wait_ge(ident_steps, 1)
            nc.gpsimd.affine_select(out=ident[:], in_=ident[:], compare_op=ALU.not_equal, fill=1.0,
                                    base=0, pattern=[[-1, P]], channel_multiplier=1).then_inc(ident_steps, 1)

            def add_products(quad, j):
                tile = (quad.n - 1) * QD + j
                ops = tile * POOL_OPS
                slot = [prod[:, (j * TILE_BANKS + i) % SLOTS, :] for i in range(TILE_BANKS)]
                pool.wait_ge(prods_done, tile * 16 + 3 * GROUP)
                wait(pool, pool_done, ops - POOL_OPS + 3)
                nc.gpsimd.tensor_tensor(sum_a[:], slot[1], slot[2], ALU.add).then_inc(pool_done, 1)
                pool.wait_ge(prods_done, tile * 16 + 4 * GROUP)
                pool.wait_ge(pool_done, ops + 1)
                nc.gpsimd.tensor_tensor(sum_a[:], sum_a[:], slot[3], ALU.add).then_inc(pool_done, 1)
                pool.wait_ge(pool_done, ops + 2)
                nc.gpsimd.tensor_tensor(sum_c[:], sum_a[:, 0:2 * UNITS], sum_a[:, 2 * UNITS:],
                                        ALU.add).then_inc(pool_done, 1)
                pool.wait_ge(pool_done, ops + 3)
                nc.gpsimd.tensor_tensor(sum_c[:], sum_c[:], slot[0][:, 2 * UNITS:],
                                        ALU.add).then_inc(pool_done, 1)
                pool.wait_ge(pool_done, ops + 4)
                pool.wait_ge(macs_done, (tile + 1) * 16)
                nc.gpsimd.tensor_tensor(sum_c[:], sum_c[:], mac[:, j % 2, :, :].rearrange("p a n -> p (a n)"),
                                        ALU.add).then_inc(pool_done, 1)
                pool.wait_ge(pool_done, ops + 5)
                if j == 0 and (not isinstance(quad.n, int) or quad.n > 1):
                    pool.wait_ge(acc2_added, quad.n)
                nc.gpsimd.tensor_tensor(cur2[:, j, :], sum_c[:, 0:UNITS], sum_c[:, UNITS:],
                                        ALU.add).then_inc(pool_done, 1)

            def mix_quad(quad, fields):
                for j in range(QD):
                    add_products(quad, j)
                    for f in fields[j::QD]:
                        gather(f)

            FIELDS_AT = [list(range(FIELDS))[i * FIELDS // (QUADS - 2):(i + 1) * FIELDS // (QUADS - 2)]
                         for i in range(QUADS)]

            def mix_batch_tile(bt, gathers):
                for q in range(QUADS):
                    if gathers and q == 0:
                        pool.wait_ge(land_copied, bt + 1)
                        pool.wait_ge(gathered, 16 * FIELDS * (bt + 1))
                        set_indices(bt + 1)
                    fields = FIELDS_AT[q] if gathers else []
                    mix_quad(Quad(bt * QUADS + q + 1, bt, q, True, True, True, False, False), fields)

            mix_batch_tile(0, True)
            with pool.Fori(1, BTILES - 1) as bt:
                mix_batch_tile(bt, True)
            mix_batch_tile(BTILES - 1, False)

        @block.scalar
        def _(act):
            for i in range(4):
                part = slice(i * W1_PART, (i + 1) * W1_PART)
                act.dma_start(w1_raw[:, part].rearrange("p (h n) -> p h n", n=UNITS),
                              w1_view[:, i * FIELDS // 4:(i + 1) * FIELDS // 4, :]).then_inc(w1_loaded[i], 16)
            act.wait_ge(select_loaded, 16)
            nc.scalar.activation(select[:], select_raw[:], ACT.Copy).then_inc(select_ready, 1)
            for i in range(4):
                part = slice(i * W1_PART, (i + 1) * W1_PART)
                act.wait_ge(w1_loaded[i], 16)
                nc.scalar.activation(w1_hi[:, part], w1_raw[:, part], ACT.Copy).then_inc(w1_hi_ready, 1)
            act.sem_inc(mlp_act, 1)
            act.wait_ge(mlp_loaded, 16 * 6)

            def multiply(quad, a):
                n = quad.n
                bank = (n - 1) * BANKS + a
                j = a // TILE_BANKS
                if a == 0 or a == BANKS // 2:
                    act.wait_ge(x0_staged, 2 * n - 1 if a == 0 else 2 * n)
                act.wait_ge(mix_done, (n - 1) * STEPS + 2 * a + 1)
                wait(act, pool_done, ((n - 1) * QD + j - 2) * POOL_OPS + (5, 1, 1, 2)[a % TILE_BANKS])
                for i in range(GROUP):
                    h = (a % TILE_BANKS) * 2 * GROUP + i
                    nc.scalar.activation(prod[:, a % SLOTS, i * UNITS:(i + 1) * UNITS],
                                         mix[(2 * a) % 4][:, i * UNITS:(i + 1) * UNITS], ACT.Copy,
                                         scale=x0[:, j, h:h + 1]).then_inc(prods_done, 1)

            def stage_quad(quad):
                n = quad.n
                act.wait_ge(land_copied, quad.bt + 1)
                wait(act, transposed, (n - 1) * ROUNDS + 1)
                wait(act, x0_staged, 2 * n)
                now = e_cur[:, bass.ds(quad.q * QD, QD), :].unsqueeze(2)
                nc.scalar.activation(e_quad[:], now.to_broadcast((P, QD, SHIFTS, FIELDS)),
                                     ACT.Copy).then_inc(quad_staged, 1)

            def stage_x0(n, half):
                act.wait_ge(quad_staged, n + 1)
                wait(act, prods_done, (n - 1) * MACS + (half + 1) * MACS // 2)
                wait(act, macs_done, (n - 1) * MACS + (half + 1) * MACS // 2)
                nc.scalar.activation(x0[:, 2 * half:2 * half + 2, :], e_quad[:, 2 * half:2 * half + 2, 0, :],
                                     ACT.Copy).then_inc(x0_staged, 1)

            def split_high(n, half):
                act.wait_ge(cur1_ready, n + 1)
                wait(act, mix_done, (n - 1) * STEPS + (half + 1) * STEPS // 2)
                cols = slice(half * 256, half * 256 + 256)
                nc.scalar.activation(cur1_hi[:, cols], cur1[:, cols], ACT.Copy).then_inc(hi_ready, 1)

            def round_fields(n):
                act.wait_ge(transposed, n * ROUNDS + 1)
                nc.scalar.activation(parts[:], trans[0][:], ACT.Copy).then_inc(parts_high, 1)
                wait(act, pairs_ready, n * CHUNKS)
                nc.scalar.activation(base_t[:], trans[0][:], ACT.Copy).then_inc(base_ready, 1)

            def round_pairs(n):
                act.wait_ge(pairs_ready, n * CHUNKS + 1)
                wait(act, layer1_done, (n - 1) * CHUNKS + 1)
                nc.scalar.activation(pair_parts[:], pairs[:, 0, :], ACT.Copy).then_inc(pairs_high, 1)

            def finish_layer1(n):
                act.wait_ge(layer1_done, (n + 1) * CHUNKS)
                wait(act, lo_ready, 2 * n)
                wait(act, acc1_added, n)
                wait(act, hi_ready, 2 * n)
                nc.scalar.activation(cur1[:], cur1_ps[:], ACT.Relu).then_inc(cur1_ready, 1)
                split_high(n, 0)

            def mlp_stage(bt, k):
                u = bt - 1
                act.wait_ge(mlp_pe, 1 + u * MLP_PE + k + 1)
                if k == 0:
                    nc.scalar.activation(in2_t[:], mlp_ps[:, 0:P], ACT.Copy).then_inc(mlp_act, 1)
                    nc.scalar.activation(in3_t[:], mlp_ps[0:DENSE, P:2 * P], ACT.Copy).then_inc(mlp_act, 1)
                elif k == 1:
                    for c in range(HID1 // P):
                        nc.scalar.activation(h1_t[:, c, :], mlp_ps[:, c * P:(c + 1) * P], ACT.Relu,
                                             bias=bias1[:, c:c + 1]).then_inc(mlp_act, 1)
                elif k == 2:
                    for c in range(HID2 // P):
                        nc.scalar.activation(h2_t[:, c, :], mlp_ps[:, c * P:(c + 1) * P], ACT.Relu,
                                             bias=bias2[:, c:c + 1]).then_inc(mlp_act, 1)
                else:
                    nc.scalar.activation(y_sb[0:1, bass.ds(u * P, P)], mlp_ps[0:1, 0:P],
                                         ACT.Copy).then_inc(mlp_act, 1)

            for quad in quads(act):
                n = quad.n
                if not quad.mixes:
                    if quad.prepares:
                        stage_quad(quad)
                        round_fields(n)
                        stage_x0(n, 0)
                        round_pairs(n)
                        finish_layer1(n)
                    else:
                        for k in range(MLP_PE):
                            mlp_stage(quad.bt, k)
                    continue
                for a in range(BANKS):
                    multiply(quad, a)
                    if a == X0_HIGH_AT:
                        stage_x0(n - 1, 1)
                        if quad.prepares:
                            stage_quad(quad)
                    if a == HIGH1_AT:
                        split_high(n - 1, 1)
                    if quad.prepares:
                        if a == ROUND_FIELDS_AT:
                            round_fields(n)
                        if a == ROUND_PAIRS_AT:
                            round_pairs(n)
                        if a == X0_LOW_AT:
                            stage_x0(n, 0)
                        if a == FINISH_AT:
                            finish_layer1(n)
                    if quad.closes and a in MLP_ACT_AT:
                        mlp_stage(quad.bt, MLP_ACT_AT.index(a))

        @block.vector
        def _(dve):
            nc.vector.memset(fold_a[:, 0, :], 0.0).then_inc(fold_zeroed, 1)
            nc.vector.memset(fold_b[:, 0, :], 0.0).then_inc(fold_zeroed, 1)
            nc.vector.memset(fold_b[0:FIELDS, 1, :], 0.0).then_inc(fold_zeroed, 1)
            nc.vector.memset(acc1[:], 0.0).then_inc(acc1_zeroed, 1)
            nc.vector.memset(acc2[:], 0.0).then_inc(acc2_zeroed, 1)
            dve.sem_inc(acc2_added, 1)
            for i in range(4):
                part = slice(i * W1_PART, (i + 1) * W1_PART)
                dve.wait_ge(w1_hi_ready, i + 1)
                nc.vector.tensor_tensor(w1_lo[:, part], w1_raw[:, part], w1_hi[:, part].bitcast(F32),
                                        ALU.subtract).then_inc(w1_lo_ready, 1)
            dve.wait_ge(fold_loaded, 16 * N_FOLD)
            dve.wait_ge(fold_zeroed, 3)
            nc.vector.tensor_tensor(w0[:], fold_a[:], fold_b[:], ALU.add).then_inc(w0_ready, 1)
            dve.wait_ge(w0_ready, 1)
            nc.vector.tensor_copy(w0_last[:], w0[:, 0, :]).then_inc(w0_ready, 1)
            dve.wait_ge(w0_ready, 2)
            third = slice(2 * FIELDS, 3 * FIELDS)
            nc.vector.tensor_tensor(w0_last[third, :], w0[third, 0, :], w0_last[third, :].bitcast(F32),
                                    ALU.subtract).then_inc(w0_ready, 1)
            dve.wait_ge(dense_loaded, 16)

            def open_batch_tile(bt):
                dve.wait_ge(gathered, 16 * FIELDS * (bt + 1))
                wait(dve, quad_staged, bt * QUADS)
                nc.vector.tensor_copy(e_cur[:],
                                      e_land[:].rearrange("p f d -> p d f")).then_inc(land_copied, 1)

            def split_fields(n):
                dve.wait_ge(base_ready, n + 1)
                low = slice(FIELDS, 2 * FIELDS)
                nc.vector.tensor_tensor(parts[low, :], base_t[low, :], parts[low, :].bitcast(F32),
                                        ALU.subtract).then_inc(parts_ready, 1)

            def multiply_pairs(n, t):
                dve.wait_ge(transposed, n * ROUNDS + t + 2)
                wait(dve, layer1_done, n * CHUNKS + max(t - 1, 0))
                nc.vector.tensor_tensor(pairs[:, t % 2, :], trans[(t + 1) % 2][:], base_t[:],
                                        ALU.mult).then_inc(pairs_ready, 1)

            def split_pairs(n):
                dve.wait_ge(pairs_high, n + 1)
                low = slice(FIELDS, 2 * FIELDS)
                nc.vector.tensor_tensor(pair_parts[low, :], pairs[low, 0, :], pair_parts[low, :].bitcast(F32),
                                        ALU.subtract).then_inc(pairs_split, 1)

            def split_low(n, half):
                dve.wait_ge(hi_ready, 2 * n + half + 1)
                wait(dve, mix_done, (n - 1) * STEPS + (half + 1) * STEPS // 2)
                cols = slice(half * 256, half * 256 + 256)
                nc.vector.tensor_tensor(cur1_lo[:, cols], cur1[:, cols], cur1_hi[:, cols].bitcast(F32),
                                        ALU.subtract).then_inc(lo_ready, 1)

            def add_acc1(n, zeroed):
                dve.wait_ge(cur1_ready, n + 1)
                dve.wait_ge(acc1_zeroed, zeroed)
                wait(dve, acc1_added, n)
                flat = acc1[:].rearrange("p j b -> p (j b)")
                nc.vector.tensor_tensor(flat, flat, cur1[:], ALU.add).then_inc(acc1_added, 1)

            def close_acc1(bt):
                dve.wait_ge(acc1_added, bt * QUADS)
                dve.wait_ge(mlp_pe, 1 + MLP_PE * (bt - 1))
                nc.vector.tensor_reduce(sum1[:], acc1[:].rearrange("p j b -> p b j"), AX,
                                        ALU.add).then_inc(acc1_closed, 1)
                if not isinstance(bt, int):
                    dve.wait_ge(acc1_closed, bt)
                    nc.vector.memset(acc1[:], 0.0).then_inc(acc1_zeroed, 1)

            def add_acc2(quad):
                n = quad.n
                dve.wait_ge(pool_done, (n - 1) * QD * POOL_OPS)
                dve.wait_ge(acc2_zeroed, quad.bt if quad.opens or quad.closes else quad.bt + 1)
                dve.wait_ge(acc2_added, n - 1)
                nc.vector.scalar_tensor_tensor(acc2[:], cur2[:], 0.0, acc2[:], ALU.max,
                                               ALU.add).then_inc(acc2_added, 1)

            def close_acc2(n, bt):
                dve.wait_ge(acc2_added, n)
                dve.wait_ge(mlp_pe, 1 + MLP_PE * (bt - 1))
                nc.vector.tensor_reduce(sum2[:], acc2[:].rearrange("p j n -> p n j"), AX,
                                        ALU.add).then_inc(acc2_closed, 1)
                nc.vector.tensor_copy(dense_now[:], dense_sb[:, bt - 1, :]).then_inc(dense_ready, 1)
                if not isinstance(bt, int):
                    dve.wait_ge(acc2_closed, bt)
                    nc.vector.memset(acc2[:], 0.0).then_inc(acc2_zeroed, 1)

            def multiply_add(n, e):
                j = e // TILE_BANKS
                if e == 0 or e == BANKS // 2:
                    dve.wait_ge(x0_staged, 2 * n - 1 if e == 0 else 2 * n)
                dve.wait_ge(mix_done, (n - 1) * STEPS + 2 * e + 2)
                if e % TILE_BANKS == 0:
                    wait(dve, pool_done, ((n - 1) * QD + j - 2) * POOL_OPS + 5)
                for i in range(GROUP):
                    k = (e % TILE_BANKS) * GROUP + i
                    h = (e % TILE_BANKS) * 2 * GROUP + GROUP + i
                    src = mix[(2 * e + 1) % 4][:, i * UNITS:(i + 1) * UNITS]
                    dst = mac[:, j % 2, i % 2, :]
                    scale = x0[:, j, h:h + 1]
                    if k < 2:
                        dve.wait_ge(prods_done, ((n - 1) * QD + j) * 16 + k + 1)
                        first = prod[:, (j * TILE_BANKS) % SLOTS, k * UNITS:(k + 1) * UNITS]
                        nc.vector.scalar_tensor_tensor(dst, src, scale, first, ALU.mult,
                                                       ALU.add).then_inc(macs_done, 1)
                    else:
                        dve.wait_ge(macs_done, (n - 1) * MACS + e * GROUP + i - 1)
                        nc.vector.scalar_tensor_tensor(dst, src, scale, dst, ALU.mult,
                                                       ALU.add).then_inc(macs_done, 1)

            for quad in quads(dve):
                n = quad.n
                if not quad.mixes:
                    if quad.prepares:
                        open_batch_tile(0)
                        split_fields(n)
                        for t in range(CHUNKS):
                            multiply_pairs(n, t)
                            if t == 0:
                                split_pairs(n)
                        split_low(n, 0)
                    else:
                        add_acc2(quad)
                        close_acc2(n, quad.bt)
                    continue
                for e in range(BANKS):
                    if e == OPEN_AT and quad.opens and quad.prepares:
                        open_batch_tile(quad.bt)
                    multiply_add(n, e)
                    if e == LOW1_AT:
                        split_low(n - 1, 1)
                    if e == ACC1_AT:
                        add_acc1(n - 1, quad.bt if quad.opens else quad.bt + 1)
                    if quad.opens and e == CLOSE1_AT:
                        close_acc1(quad.bt)
                    if quad.sums and e == ACC2_AT:
                        add_acc2(quad)
                    if quad.closes and e == CLOSE2_AT:
                        close_acc2(n, quad.bt)
                    if quad.prepares:
                        if e == SPLIT_AT:
                            split_fields(n)
                        if e in PAIRS_AT:
                            multiply_pairs(n, PAIRS_AT.index(e))
                        if e == SPLIT_PAIRS_AT:
                            split_pairs(n)
                        if e == LOW0_AT:
                            split_low(n, 0)

        @block.tensor
        def _(pe):
            def transpose_fields(n):
                pe.wait_ge(quad_staged, n + 1)
                wait(pe, pairs_ready, n * CHUNKS - 1)
                for d in range(QD):
                    op = nc.tensor.transpose(trans[0][:, d * P:(d + 1) * P],
                                             e_quad[:, d, :, :].rearrange("p c f -> p (c f)"), ident[:])
                op.then_inc(transposed, 1)

            def place_fields(n, r):
                if r == 1:
                    pe.wait_ge(parts_ready, n + 1)
                    wait(pe, pairs_ready, n * CHUNKS)
                elif r == 2:
                    pe.wait_ge(base_ready, n + 1)
                else:
                    pe.wait_ge(pairs_ready, n * CHUNKS + r - 2)
                nc.tensor.matmul(trans[r % 2][:], select[:, r - 1, :], parts[:],
                                 start=True, stop=True).then_inc(transposed, 1)

            def layer1(n, t):
                if t == 0:
                    pe.wait_ge(pairs_split, n + 1)
                    wait(pe, cur1_ready, n)
                    weights, moving = w0_last[:], pair_parts[:]
                else:
                    pe.wait_ge(pairs_ready, n * CHUNKS + t + 1)
                    weights, moving = w0[:, t, :], pairs[:, t % 2, :]
                nc.tensor.matmul(cur1_ps[:], weights, moving,
                                 start=(t == 0), stop=(t == CHUNKS - 1)).then_inc(layer1_done, 1)

            def layer2(n, s):
                j, k = divmod(s, STEPS // QD)
                if k == 0 and j % 2 == 0:
                    pe.wait_ge(lo_ready, 2 * n - 1 if j == 0 else 2 * n)
                bank = (n - 1) * BANKS + s // 2
                wait(pe, macs_done if s % 2 else prods_done, (bank - 1) * GROUP)
                hi, lo = cur1_hi[:, j * P:(j + 1) * P], cur1_lo[:, j * P:(j + 1) * P]
                cols = slice(k * GROUP * UNITS, (k + 1) * GROUP * UNITS)
                nc.tensor.matmul(mix[s % 4][:], hi, w1_hi[:, cols], start=True, stop=False)
                nc.tensor.matmul(mix[s % 4][:], hi, w1_lo[:, cols], start=False, stop=False)
                nc.tensor.matmul(mix[s % 4][:], lo, w1_hi[:, cols], start=False, stop=True).then_inc(mix_done, 1)

            def mlp_stage(bt, k):
                u = bt - 1
                if k == 0:
                    pe.wait_ge(acc2_closed, bt)
                    pe.wait_ge(dense_ready, bt)
                    pe.wait_ge(mlp_act, 1 + u * MLP_ACT)
                    nc.tensor.transpose(mlp_ps[:, 0:P], sum2[:], ident[:])
                    nc.tensor.transpose(mlp_ps[0:DENSE, P:2 * P], dense_now[:], ident[:]).then_inc(mlp_pe, 1)
                elif k == 1:
                    pe.wait_ge(acc1_closed, bt)
                    pe.wait_ge(mlp_act, 1 + u * MLP_ACT + 2)
                    for c in range(HID1 // P):
                        cols = slice(c * P, (c + 1) * P)
                        nc.tensor.matmul(mlp_ps[:, cols], top1[:, 0, cols], sum1[:], start=True, stop=False)
                        nc.tensor.matmul(mlp_ps[:, cols], top1[:, 1, cols], in2_t[:], start=False, stop=False)
                        op = nc.tensor.matmul(mlp_ps[:, cols], top1_d[:, cols], in3_t[:], start=False, stop=True)
                    op.then_inc(mlp_pe, 1)
                elif k == 2:
                    pe.wait_ge(mlp_act, 1 + u * MLP_ACT + 6)
                    for c in range(HID2 // P):
                        cols = slice(c * P, (c + 1) * P)
                        for i in range(HID1 // P):
                            op = nc.tensor.matmul(mlp_ps[:, cols], top2[:, i, cols], h1_t[:, i, :],
                                                  start=(i == 0), stop=(i == HID1 // P - 1))
                    op.then_inc(mlp_pe, 1)
                else:
                    pe.wait_ge(mlp_act, 1 + u * MLP_ACT + 8)
                    for i in range(HID2 // P):
                        op = nc.tensor.matmul(mlp_ps[0:1, 0:P], top3[:, i:i + 1], h2_t[:, i, :],
                                              start=(i == 0), stop=(i == HID2 // P - 1))
                    op.then_inc(mlp_pe, 1)

            pe.sem_inc(mlp_pe, 1)
            pe.wait_ge(ident_steps, 2)
            for quad in quads(pe):
                n = quad.n
                if not quad.mixes:
                    if quad.prepares:
                        pe.wait_ge(w0_ready, 3)
                        transpose_fields(n)
                        pe.wait_ge(select_ready, 1)
                        for r in range(1, ROUNDS):
                            place_fields(n, r)
                            if r >= 2:
                                layer1(n, r - 2)
                        layer1(n, CHUNKS - 1)
                        pe.wait_ge(w1_lo_ready, 4)
                        pe.wait_ge(mlp_loaded, 16 * 6)
                    else:
                        for k in range(MLP_PE):
                            mlp_stage(quad.bt, k)
                    continue
                for s in range(STEPS):
                    if quad.prepares and s in ROUND_AT:
                        if s == ROUND_AT[0]:
                            transpose_fields(n)
                        else:
                            place_fields(n, ROUND_AT.index(s))
                    if quad.prepares and s in LAYER1_AT:
                        layer1(n, LAYER1_AT.index(s))
                    if quad.closes and s in MLP_PE_AT:
                        mlp_stage(quad.bt, MLP_PE_AT.index(s))
                    layer2(n, s)


def kernel(**inputs):
    import concourse.bacc as bacc
    from concourse.bass_utils import run_bass_kernel_spmd

    nc = bacc.Bacc("TRN2", target_bir_lowering=False, num_devices=1)
    names = (["dense_ctx", "ids"] + [f"tbl_{f}" for f in range(FIELDS)]
             + ["W_top1", "b_top1", "W_top2", "b_top2", "W_top3", "L0_rec_filter_0", "L0_rec_filter_1"])
    arrays, aps = {}, {}
    for name in names:
        a = np.ascontiguousarray(inputs[name])
        arrays[f"in_{name}"] = a
        aps[name] = nc.dram_tensor(f"in_{name}", a.shape, mybir.dt.from_np(a.dtype), kind="ExternalInput").ap()
    arrays["selection"] = selection_matrices()
    selection = nc.dram_tensor("selection", arrays["selection"].shape, F32, kind="ExternalInput").ap()
    out = nc.dram_tensor("out_y", (BATCH, 1), F32, kind="ExternalOutput").ap()
    build_program(nc, aps["dense_ctx"], aps["ids"], [aps[f"tbl_{f}"] for f in range(FIELDS)],
                  aps["W_top1"], aps["b_top1"], aps["W_top2"], aps["b_top2"], aps["W_top3"],
                  aps["L0_rec_filter_0"], aps["L0_rec_filter_1"], selection, out)
    result = run_bass_kernel_spmd(nc, [arrays], core_ids=[0])
    return result.results[0]["out_y"]
```
